# Optimizing a Trainium2 kernel written in Bass

```python
import numpy as np
import jax
import jax.numpy as jnp

def _softmax(x, axis=-1):
    return jax.nn.softmax(x, axis=axis)

def _gelu(x):
    return jax.nn.gelu(x, approximate=True)

def _silu(x):
    return jax.nn.silu(x)

def _sigmoid(x):
    return jax.nn.sigmoid(x)

def _layernorm(x, axis=-1, eps=1e-05):
    m = jnp.mean(x, axis=axis, keepdims=True)
    v = jnp.var(x, axis=axis, keepdims=True)
    return (x - m) / jnp.sqrt(v + eps)

def _scatter_add(tgt, idx, src, axis=0):
    return tgt.at[idx].add(src)

def _segment_sum(src, seg, n):
    return jax.ops.segment_sum(src, seg, n)
kernel_name = 'mk_lm_tower_d1_tok_ids1024_r4_e821d6'

def setup_inputs(seed: int=0):
    np.random.seed(seed)
    _w = jnp.asarray

    def _rec_inputs():
        import jax
        import jax.numpy as jnp
        _rk = jax.random.key(seed)
        x = jax.random.randint(jax.random.fold_in(_rk, 1), (8, 512), 0, 2048, jnp.int32)
        return x
    x = _rec_inputs()

    def _L0_tok_setup():
        import jax, jax.numpy as jnp
        import numpy as np
        CODEBOOK_SIZE = 2048
        CODEBOOK_DIM = 256
        HIDDEN_DIM = 1024
        OUT_DIM = 256
        B, M = (32, 144)
        key = jax.random.key(seed)
        k_idx, k_cb, k_w1, k_w2 = jax.random.split(key, 4)
        index = jax.random.randint(k_idx, (B, M), 0, CODEBOOK_SIZE, dtype=jnp.int32)
        codebook = CODEBOOK_DIM ** 0.5 * jax.random.normal(k_cb, (CODEBOOK_SIZE, CODEBOOK_DIM), dtype=jnp.float32)
        s1 = 1.0 / np.sqrt(CODEBOOK_DIM)
        s2 = 1.0 / np.sqrt(HIDDEN_DIM)
        W1 = s1 * jax.random.normal(k_w1, (CODEBOOK_DIM, HIDDEN_DIM), dtype=jnp.float32)
        b1 = jnp.zeros((HIDDEN_DIM,), dtype=jnp.float32)
        W2 = s2 * jax.random.normal(k_w2, (HIDDEN_DIM, OUT_DIM), dtype=jnp.float32)
        b2 = jnp.zeros((OUT_DIM,), dtype=jnp.float32)
        return {'index': index, 'codebook': codebook, 'W1': W1, 'b1': b1, 'W2': W2, 'b2': b2}
    _L0_tok_all = _L0_tok_setup()
    _L0_tok_in = {k: v for k, v in _L0_tok_all.items() if k in ('codebook', 'W1', 'b1', 'W2', 'b2')}
    del _L0_tok_all

    def _L0_attn_setup():
        import jax, jax.numpy as jnp
        import numpy as np
        B, T = (2, 512)
        TOK, POS = (128, 128)
        H, D, KVH = (16, 64, 4)
        key = jax.random.key(seed)
        ks = jax.random.split(key, 7)

        def w(k, shape, fan_in):
            return jax.random.normal(k, shape, jnp.float32) / np.float32(np.sqrt(fan_in))
        x = jax.random.normal(ks[0], (B, T, TOK + POS), jnp.float32)
        Wq = w(ks[1], (POS, H * D), POS)
        Wk = w(ks[2], (POS, KVH * D), POS)
        Wv = w(ks[3], (TOK, KVH * D), TOK)
        Wo = w(ks[4], (H * D, TOK + POS), H * D)
        q_phase_angle = 0.1 * jax.random.normal(ks[5], (H,), jnp.float32)
        alibi_log_slopes = jnp.full((H,), np.float32(np.log(np.log(10.0))))
        return dict(x=x, Wq=Wq, Wk=Wk, Wv=Wv, Wo=Wo, q_phase_angle=q_phase_angle, alibi_log_slopes=alibi_log_slopes)
    _L0_attn_all = _L0_attn_setup()
    _L0_attn_in = {k: v for k, v in _L0_attn_all.items() if k in ('Wq', 'Wk', 'Wv', 'Wo', 'q_phase_angle', 'alibi_log_slopes')}
    del _L0_attn_all

    def _L0_ffn_setup():
        import jax, jax.numpy as jnp
        import numpy as np
        D_MODEL, D_FF, RANK = (256, 1024, 64)
        B, S = (4, 1024)
        key = jax.random.key(seed)
        ks = jax.random.split(key, 7)
        return {'x': jax.random.normal(ks[0], (B, S, D_MODEL), dtype=jnp.float32), 'U1': jax.random.normal(ks[1], (D_MODEL, RANK), dtype=jnp.float32) * 0.02, 'V1': jax.random.normal(ks[2], (RANK, D_FF), dtype=jnp.float32) * 0.02, 'b1': jnp.zeros((D_FF,), dtype=jnp.float32), 'U2': jax.random.normal(ks[3], (D_FF, RANK), dtype=jnp.float32) * 0.02, 'V2': jax.random.normal(ks[4], (RANK, D_MODEL), dtype=jnp.float32) * 0.02, 'b2': jnp.zeros((D_MODEL,), dtype=jnp.float32)}
    _L0_ffn_all = _L0_ffn_setup()
    _L0_ffn_in = {k: v for k, v in _L0_ffn_all.items() if k in ('U1', 'V1', 'b1', 'U2', 'V2', 'b2')}
    del _L0_ffn_all
    return {'x': x, 'L0_tok_codebook': _L0_tok_in['codebook'], 'L0_tok_W1': _L0_tok_in['W1'], 'L0_tok_b1': _L0_tok_in['b1'], 'L0_tok_W2': _L0_tok_in['W2'], 'L0_tok_b2': _L0_tok_in['b2'], 'L0_attn_Wq': _L0_attn_in['Wq'], 'L0_attn_Wk': _L0_attn_in['Wk'], 'L0_attn_Wv': _L0_attn_in['Wv'], 'L0_attn_Wo': _L0_attn_in['Wo'], 'L0_attn_q_phase_angle': _L0_attn_in['q_phase_angle'], 'L0_attn_alibi_log_slopes': _L0_attn_in['alibi_log_slopes'], 'L0_ffn_U1': _L0_ffn_in['U1'], 'L0_ffn_V1': _L0_ffn_in['V1'], 'L0_ffn_b1': _L0_ffn_in['b1'], 'L0_ffn_U2': _L0_ffn_in['U2'], 'L0_ffn_V2': _L0_ffn_in['V2'], 'L0_ffn_b2': _L0_ffn_in['b2']}

def reference(x, L0_tok_codebook, L0_tok_W1, L0_tok_b1, L0_tok_W2, L0_tok_b2, L0_attn_Wq, L0_attn_Wk, L0_attn_Wv, L0_attn_Wo, L0_attn_q_phase_angle, L0_attn_alibi_log_slopes, L0_ffn_U1, L0_ffn_V1, L0_ffn_b1, L0_ffn_U2, L0_ffn_V2, L0_ffn_b2):
    import jax
    import jax.numpy as jnp

    def _L0_tok_ref(index, codebook, W1, b1, W2, b2):
        import jax, jax.numpy as jnp
        import numpy as np
        CODEBOOK_SIZE = 2048
        CODEBOOK_DIM = 256
        HIDDEN_DIM = 1024
        OUT_DIM = 256
        B, M = (32, 144)
        quantized = jnp.take(codebook, index, axis=0)
        h = jax.nn.gelu(jnp.einsum('bmd,dh->bmh', quantized, W1) + b1)
        rec = jnp.einsum('bmh,ho->bmo', h, W2) + b2
        return rec

    def _L0_attn_ref(x, Wq, Wk, Wv, Wo, q_phase_angle, alibi_log_slopes):
        import jax, jax.numpy as jnp
        import numpy as np
        B, T = (2, 512)
        TOK, POS = (128, 128)
        H, D, KVH = (16, 64, 4)
        b, t, _ = x.shape
        x_tok = x[:, :, :TOK]
        x_pos = x[:, :, TOK:]
        q = (x_pos @ Wq).reshape(b, t, H, D).transpose(0, 2, 1, 3)
        k = (x_pos @ Wk).reshape(b, t, KVH, D).transpose(0, 2, 1, 3)
        v = (x_tok @ Wv).reshape(b, t, KVH, D).transpose(0, 2, 1, 3)
        c = jnp.cos(q_phase_angle)[None, :, None, None]
        s = jnp.sin(q_phase_angle)[None, :, None, None]
        q2 = q.reshape(b, H, t, D // 2, 2)
        q0, q1 = (q2[..., 0], q2[..., 1])
        q = jnp.stack([q0 * c - q1 * s, q0 * s + q1 * c], axis=-1).reshape(b, H, t, D)
        rep = H // KVH
        k = jnp.repeat(k, rep, axis=1)
        v = jnp.repeat(v, rep, axis=1)
        att = jnp.einsum('bhqd,bhkd->bhqk', q, k) / np.float32(np.sqrt(D))
        pos = jnp.arange(t)
        rel = (pos[:, None] - pos[None, :]).astype(jnp.float32)
        att = att + jnp.exp(alibi_log_slopes)[None, :, None, None] * rel[None, None]
        mask = pos[:, None] >= pos[None, :]
        att = jnp.where(mask[None, None], att, -jnp.inf)
        m = jnp.max(att, axis=-1, keepdims=True)
        e = jnp.exp(att - m)
        att = e / (1.0 + jnp.sum(e, axis=-1, keepdims=True))
        out = jnp.einsum('bhqk,bhkd->bhqd', att, v)
        out = out.transpose(0, 2, 1, 3).reshape(b, t, H * D)
        return out @ Wo

    def _L0_ffn_ref(x, U1, V1, b1, U2, V2, b2):
        import jax, jax.numpy as jnp
        import numpy as np
        D_MODEL, D_FF, RANK = (256, 1024, 64)
        B, S = (4, 1024)
        P = jnp.einsum('bsd,dr->bsr', x, U1)
        H = jax.nn.gelu(jnp.einsum('bsr,rf->bsf', P, V1) + b1)
        Q = jnp.einsum('bsf,fr->bsr', H, U2)
        return jnp.einsum('bsr,rd->bsd', Q, V2) + b2
    h = _L0_tok_ref(x, L0_tok_codebook, L0_tok_W1, L0_tok_b1, L0_tok_W2, L0_tok_b2)
    h = h + _L0_attn_ref(_layernorm(h, axis=-1), L0_attn_Wq, L0_attn_Wk, L0_attn_Wv, L0_attn_Wo, L0_attn_q_phase_angle, L0_attn_alibi_log_slopes)
    h = h + _L0_ffn_ref(_layernorm(h, axis=-1), L0_ffn_U1, L0_ffn_V1, L0_ffn_b1, L0_ffn_U2, L0_ffn_V2, L0_ffn_b2)
    return h

_drawn_inputs = setup_inputs


def setup_inputs(seed=0):
    import zlib

    import numpy as np

    out = dict(_drawn_inputs(seed))
    spreads = {'L0_tok_b1': (0.0, 0.8),
     'L0_tok_b2': (0.0, 0.8),
     'L0_attn_alibi_log_slopes': (0.834032416343689, 0.6),
     'L0_ffn_b1': (0.0, 0.8),
     'L0_ffn_b2': (0.0, 0.8)}
    factors = {'L0_attn_Wq': 8.0,
     'L0_attn_Wk': 8.0,
     'L0_attn_q_phase_angle': 8.0,
     'L0_ffn_U1': 8.0,
     'L0_ffn_V1': 8.0,
     'L0_ffn_U2': 8.0,
     'L0_ffn_V2': 8.0}
    for name, (base, spread) in spreads.items():
        noise = np.random.default_rng([zlib.crc32(name.encode()), seed]).standard_normal(out[name].shape)
        drawn = base * np.exp(spread * noise) if base else spread * noise
        out[name] = jnp.asarray(drawn.astype(out[name].dtype))
    for name, factor in factors.items():
        out[name] = (out[name] * factor).astype(out[name].dtype)
    return out
```

```python
import concourse.bass as bass
from concourse import mybir
from contextlib import ExitStack

F32 = mybir.dt.float32
F32R = mybir.dt.float32r
I32 = mybir.dt.int32
U32 = mybir.dt.uint32
ALU = mybir.AluOpType
ACT = mybir.ActivationFunctionType

P = 128
ROWS, DIM, HID = 2048, 256, 1024
B, T = 8, 512
NT = T // P
HEADS, D, KVH = 16, 64, 4
REP = HEADS // KVH
PAIRS = HEADS // 2
RANK, FF = 64, 1024
KD = DIM // P
KH = HID // P
KF = FF // P
EPS = 1e-5
TRI = T * (NT + 1) // 2
MASKED = 1e30
LEAST_SLOPE = 1e-10

Q_AT = {3: 0, 0: 512, 2: 640, 1: 1024}
K_AT = {0: 0, 1: 512, 3: 896, 2: 1024}
Q_ORDER = (3, 2, 0, 1)
Q_BANK = {3: 1, 2: 2, 0: 2, 1: 3}
BANKS = 3


class Count:

    def __init__(self, sem, per, first=0):
        self.sem, self.per, self.first = sem, per, first

    def at(self, i, k):
        return i * self.per + (k + self.first)


def bank_waits(uses, released):
    order = {name: k + 1 for k, name in enumerate(released)}
    last = {bank: order[name] - len(released) for name, bank in uses}
    out = {}
    for name, bank in uses:
        out[name] = last[bank]
        last[bank] = order[name]
    return out


def lm_tower(nc, x, codebook, W1, b1, W2, b2, Wq, Wk, Wv, Wo, angle, log_slope, U1, V1, c1, U2, V2, c2, out):
    table = nc.dram_tensor("token_table", (ROWS, DIM), F32, kind="Internal").ap()
    with ExitStack() as ctx:
        def sem(name):
            return ctx.enter_context(nc.semaphore(name))

        def sb(name, shape, dt=F32):
            return ctx.enter_context(nc.sbuf_tensor(name, shape, dt))

        ident = sb("ident", [P, P])
        causal = sb("causal", [P, TRI])
        slope = sb("slope", [P, HEADS])
        wq_hi, wq_lo = sb("wq_hi", [P, HEADS, 2, D], F32R), sb("wq_lo", [P, HEADS, 2, D], F32R)
        wk_hi, wk_lo = sb("wk_hi", [P, KVH, 2, D], F32R), sb("wk_lo", [P, KVH, 2, D], F32R)
        wv_hi, wv_lo = sb("wv_hi", [P, KVH * D], F32R), sb("wv_lo", [P, KVH * D], F32R)
        wo_hi, wo_lo = sb("wo_hi", [P, PAIRS, DIM], F32R), sb("wo_lo", [P, PAIRS, DIM], F32R)
        u1_hi, u1_lo = sb("u1_hi", [P, KD, 2, RANK], F32R), sb("u1_lo", [P, KD, 2, RANK], F32R)
        v1_hi, v1_lo = sb("v1_hi", [P, FF], F32R), sb("v1_lo", [P, FF], F32R)
        u2_both = sb("u2_both", [P, KF, 2 * RANK], F32R)
        v2_hi, v2_lo = sb("v2_hi", [P, DIM], F32R), sb("v2_lo", [P, DIM], F32R)
        c1_col = sb("c1_col", [P, KF])
        c2_row = sb("c2_row", [P, DIM])

        ps = ctx.enter_context(nc.psum_tensor("ps", [P, 8 * 512], F32))
        score_ps = ps[:, 0:TRI]
        turn_ps = ps[:, 3 * 512:3 * 512 + TRI]

        def a_bank(n):
            return ps[:, (3 + n) * 512:(4 + n) * 512]

        def v_bank(n):
            return ps[:, (6 + n) * 512:(7 + n) * 512]

        with ExitStack() as part:
            token_table(nc, part, locals())
        with ExitStack() as part:
            layer(nc, part, locals())


def token_table(nc, part, env):
    g = env
    ps, a_bank, v_bank, ident, causal = g["ps"], g["a_bank"], g["v_bank"], g["ident"], g["causal"]

    def sem(name):
        return part.enter_context(nc.semaphore(name))

    def sb(name, shape, dt=F32):
        return part.enter_context(nc.sbuf_tensor(name, shape, dt))

    CH = 512
    NC = ROWS // CH
    w1_f, w2_f = sb("w1_f", [P, KD, HID]), sb("w2_f", [P, KH, DIM])
    w1_hi, w1_lo = sb("w1_hi", [P, KD, HID], F32R), sb("w1_lo", [P, KD, HID], F32R)
    w2_hi, w2_lo = sb("w2_hi", [P, KH, DIM], F32R), sb("w2_lo", [P, KH, DIM], F32R)
    b1_col, b2_row = sb("b1_col", [P, KH]), sb("b2_row", [P, DIM])
    wq_f, rot, rot2 = sb("wq_f", [P, HEADS * D]), sb("rot", [P, HEADS * D]), sb("rot2", [P, HEADS * D])
    wk_f, wv_f, wo_f = sb("wk_f", [P, KVH * D]), sb("wv_f", [P, KVH * D]), sb("wo_f", [P, PAIRS, DIM])
    u1_f, v1_f, u2_f, v2_f = (sb("u1_f", [P, KD, RANK]), sb("v1_f", [P, FF]), sb("u2_f", [P, KF, RANK]),
                              sb("v2_f", [P, DIM]))
    ang, turns_i, turns = sb("ang", [P, HEADS]), sb("turns_i", [P, HEADS], I32), sb("turns", [P, HEADS])
    sin_t, half, cos_t, inv = sb("sin_t", [P, HEADS]), sb("half", [P, HEADS]), sb("cos_t", [P, HEADS]), sb("inv", [P, HEADS])
    ls = sb("ls", [P, HEADS])
    key_i = sb("key_i", [P, T], I32)
    rows = sb("rows", [P, NT, DIM])
    ct_hi, ct_lo = sb("ct_hi", [P, KD, CH], F32R), sb("ct_lo", [P, KD, CH], F32R)
    hid = sb("hid", [P, 2, CH])
    hid_hi, hid_lo = sb("hid_hi", [P, KH, CH], F32R), sb("hid_lo", [P, KH, CH], F32R)
    made = sb("made", [P, NT, DIM])

    w1_in, w2_in, b_in, rows_in, ang_in, rest_in = (sem("w1_in"), sem("w2_in"), sem("b_in"), sem("rows_in"),
                                                    sem("ang_in"), sem("rest_in"))
    w1_hi_done, w2_hi_done, w_done = sem("w1_hi_done"), sem("w2_hi_done"), sem("w_done")
    ident_done, pool_step, v_step, trig_in, trig_out = (sem("ident_done"), sem("pool_step"), sem("v_step"),
                                                        sem("trig_in"), sem("trig_out"))
    stored = sem("stored")

    v_uses = [("ct0", 0), ("ct1", 1), ("row0", 0), ("row1", 1)]
    v_wait = bank_waits(v_uses, [n for n, _ in v_uses])
    a_wait = bank_waits([(m, m % 3) for m in range(KH)], range(KH))
    ct_full, ct_hi_done, v_free = Count(sem("ct_full"), 2), Count(sem("ct_hi_done"), 2), Count(sem("v_free"), 4, 2)
    hid_full, hid_made, hid_split = Count(sem("hid_full"), KH), Count(sem("hid_made"), KH, 3), Count(sem("hid_split"), KH, 2)
    hid_hi_done = Count(sem("hid_hi_done"), KH)
    row_full, stores = Count(sem("row_full"), 2), Count(stored, 16, 16)
    rows_free, rows_got = Count(sem("rows_free"), 1, 1), Count(rows_in, 16)

    def twice(t, n):
        return t.rearrange("p (n d) -> p n d", n=n).unsqueeze(2).broadcast_to([P, n, 2, D])

    with nc.Block() as block:
        @block.sync
        def _(sp):
            sp.sem_inc(stored, 16)
            sp.dma_start(w1_f[:, :, :], g["W1"].rearrange("(k p) n -> p k n", p=P)).then_inc(w1_in, 16)
            sp.dma_start(b1_col[:, :], g["b1"].rearrange("(k p) -> p k", p=P), allow_slow_non_contiguous=True).then_inc(b_in, 16)
            sp.dma_start(b2_row[:, :], g["b2"].partition_broadcast(P)).then_inc(b_in, 16)
            sp.dma_start(w2_f[:, :, :], g["W2"].rearrange("(k p) n -> p k n", p=P)).then_inc(w2_in, 16)
            with nc.sync.Fori(0, NC) as i:
                sp.wait_ge(rows_free.sem, rows_free.at(i, 0))
                sp.dma_start(rows[:, :, :], g["codebook"][bass.ds(i * CH, CH), :].rearrange("(t p) n -> p t n", p=P))\
                    .then_inc(rows_in, 16)
                sp.wait_ge(v_free.sem, v_free.at(i, 4))
                sp.dma_start(g["table"][bass.ds(i * CH, CH), :].rearrange("(t p) n -> p t n", p=P), made[:, :, :])\
                    .then_inc(stored, 16)
            sp.wait_ge(stored, 16 * NC + 16)

        @block.gpsimd
        def _(pool):
            pool.dma_start(ang[:, :], g["angle"].partition_broadcast(P)).then_inc(ang_in, 16)
            pool.dma_start(ls[:, :], g["log_slope"].partition_broadcast(P)).then_inc(ang_in, 16)
            pool.dma_start(wq_f[:, :], g["Wq"]).then_inc(ang_in, 16)
            pool.dma_start(wk_f[:, :], g["Wk"]).then_inc(rest_in, 16)
            pool.dma_start(wv_f[:, :], g["Wv"]).then_inc(rest_in, 16)
            pool.dma_start(wo_f[:, :, :], g["Wo"].rearrange("(k p) n -> p k n", p=P)).then_inc(rest_in, 16)
            pool.dma_start(u1_f[:, :, :], g["U1"].rearrange("(k p) n -> p k n", p=P)).then_inc(rest_in, 16)
            pool.dma_start(v1_f[0:RANK, :], g["V1"]).then_inc(rest_in, 16)
            pool.dma_start(v1_f[RANK:P, :], g["V1"]).then_inc(rest_in, 16)
            pool.dma_start(u2_f[:, :, :], g["U2"].rearrange("(k p) n -> p k n", p=P)).then_inc(rest_in, 16)
            pool.dma_start(v2_f[0:RANK, :], g["V2"]).then_inc(rest_in, 16)
            pool.dma_start(v2_f[RANK:P, :], g["V2"]).then_inc(rest_in, 16)
            pool.dma_start(g["c1_col"][:, :], g["c1"].rearrange("(k p) -> p k", p=P), allow_slow_non_contiguous=True).then_inc(rest_in, 16)
            pool.dma_start(g["c2_row"][:, :], g["c2"].partition_broadcast(P)).then_inc(rest_in, 16)
            steps = [0]

            def step(ins):
                steps[0] += 1
                ins.then_inc(pool_step, 1)
                pool.wait_ge(pool_step, steps[0])

            step(pool.memset(ident[:, :], 0.0))
            pool.affine_select(out=ident[:, :], in_=ident[:, :], compare_op=ALU.not_equal, fill=1.0, base=0,
                               pattern=[[-1, P]], channel_multiplier=1).then_inc(ident_done, 1)
            step(pool.iota(key_i[:, :], pattern=[[1, T]], base=0, channel_multiplier=0))
            for q in range(NT):
                n = P * (q + 1)
                step(pool.tensor_copy(causal[:, Q_AT[q]:Q_AT[q] + n], key_i[:, 0:n]))
                step(pool.affine_select(out=causal[:, Q_AT[q]:Q_AT[q] + n], in_=causal[:, Q_AT[q]:Q_AT[q] + n],
                                        compare_op=ALU.is_ge, fill=MASKED, base=P * q, pattern=[[-1, n]],
                                        channel_multiplier=1))
            pool.wait_ge(rest_in, 16 * 11)
            flat = lambda t: t[:, :, :].rearrange("p a b -> p (a b)")
            for hi, lo, full in ((g["wk_hi"][:, :, :, :], g["wk_lo"][:, :, :, :], twice(wk_f[:, :], KVH)), (g["wv_hi"][:, :], g["wv_lo"][:, :], wv_f[:, :]),
                                 (flat(g["wo_hi"]), flat(g["wo_lo"]), flat(wo_f)), (g["u1_hi"][:, :, :, :], g["u1_lo"][:, :, :, :], twice(flat(u1_f), KD)),
                                 (g["v1_hi"][:, :], g["v1_lo"][:, :], v1_f[:, :]),
                                 (g["u2_both"][:, :, 0:RANK], g["u2_both"][:, :, RANK:2 * RANK], u2_f[:, :, :]),
                                 (g["v2_hi"][:, :], g["v2_lo"][:, :], v2_f[:, :])):
                step(pool.tensor_scalar(hi, full, 1.0, 1.0, ALU.mult, ALU.mult))
                step(pool.tensor_tensor(lo, full, hi.bitcast(F32), ALU.subtract))

        @block.scalar
        def _(act):
            act.sem_inc(hid_made.sem, 3)
            act.wait_ge(w1_in, 16)
            for k in range(KD):
                act.activation(w1_hi[:, k, :], w1_f[:, k, :], ACT.Copy).then_inc(w1_hi_done, 1)
            act.wait_ge(trig_in, 1)
            act.activation(sin_t[:, :], ang[:, :], ACT.Sin).then_inc(trig_out, 1)
            act.activation(half[:, :], ang[:, :], ACT.Sin, scale=0.5).then_inc(trig_out, 1)
            act.activation(g["slope"][:, :], ls[:, :], ACT.Exp).then_inc(trig_out, 1)
            act.wait_ge(w2_in, 16)
            for k in range(2):
                act.activation(w2_hi[:, 4 * k:4 * k + 4, :], w2_f[:, 4 * k:4 * k + 4, :], ACT.Copy).then_inc(w2_hi_done, 1)
            act.wait_ge(b_in, 32)
            with nc.scalar.Fori(0, NC) as i:
                for k in range(KD):
                    act.wait_ge(ct_full.sem, ct_full.at(i, k + 1))
                    act.activation(ct_hi[:, k, :], v_bank(k), ACT.Copy).then_inc(ct_hi_done.sem, 1)
                for m in range(KH):
                    act.wait_ge(hid_split.sem, hid_split.at(i, m - 1))
                    act.wait_ge(hid_full.sem, hid_full.at(i, m + 1))
                    act.activation(hid[:, m % 2, :], a_bank(m % 3), ACT.Gelu_apprx_tanh, bias=b1_col[:, m:m + 1])\
                        .then_inc(hid_made.sem, 1)

        @block.vector
        def _(dve):
            steps = [0]

            def step(ins):
                steps[0] += 1
                ins.then_inc(v_step, 1)
                dve.wait_ge(v_step, steps[0])

            dve.sem_inc(v_free.sem, 2)
            dve.sem_inc(hid_split.sem, 2)
            dve.wait_ge(w1_in, 16)
            for k in range(KD):
                dve.wait_ge(w1_hi_done, k + 1)
                dve.tensor_tensor(w1_lo[:, k, :], w1_f[:, k, :], w1_hi[:, k, :].bitcast(F32), ALU.subtract)\
                    .then_inc(w_done, 1)
            dve.wait_ge(ang_in, 48)
            step(dve.tensor_scalar(turns_i[:, :], ang[:, :], 0.15915494309189535, None, ALU.mult))
            step(dve.tensor_copy(turns[:, :], turns_i[:, :]))
            for part_of_turn in (6.28125, 1.93500518798828125e-3, 3.01991598e-7):
                step(dve.scalar_tensor_tensor(ang[:, :], turns[:, :], -part_of_turn, ang[:, :], ALU.mult, ALU.add))
            dve.tensor_scalar(ang[:, :], ang[:, :], 3.1415925, -3.1415925, ALU.min, ALU.max).then_inc(trig_in, 1)
            dve.wait_ge(w2_in, 16)
            for k in range(2):
                dve.wait_ge(w2_hi_done, k + 1)
                dve.tensor_tensor(w2_lo[:, 4 * k:4 * k + 4, :], w2_f[:, 4 * k:4 * k + 4, :],
                                  w2_hi[:, 4 * k:4 * k + 4, :].bitcast(F32), ALU.subtract).then_inc(w_done, 1)
            dve.wait_ge(trig_out, 3)
            step(dve.tensor_tensor(cos_t[:, :], half[:, :], half[:, :], ALU.mult))
            step(dve.tensor_scalar(cos_t[:, :], cos_t[:, :], -2.0, 1.0, ALU.mult, ALU.add))
            step(dve.tensor_scalar(g["slope"][:, :], g["slope"][:, :], LEAST_SLOPE, None, ALU.max))
            step(dve.reciprocal(inv[:, :], g["slope"][:, :]))
            step(dve.tensor_scalar(inv[:, :], inv[:, :], -float(D) ** -0.5, None, ALU.mult))
            step(dve.tensor_tensor(cos_t[:, :], cos_t[:, :], inv[:, :], ALU.mult))
            step(dve.tensor_tensor(sin_t[:, :], sin_t[:, :], inv[:, :], ALU.mult))
            pairs = lambda t, e: t[:, :].rearrange("p (h d e) -> p h d e", h=HEADS, e=2)[:, :, :, e]
            wide = lambda t: t[:, :].unsqueeze(2).broadcast_to([P, HEADS, D // 2])
            step(dve.tensor_tensor(pairs(rot, 0), pairs(wq_f, 0), wide(cos_t), ALU.mult))
            step(dve.tensor_tensor(pairs(rot2, 0), pairs(wq_f, 1), wide(sin_t), ALU.mult))
            step(dve.tensor_tensor(pairs(rot, 1), pairs(wq_f, 0), wide(sin_t), ALU.mult))
            step(dve.tensor_tensor(pairs(rot2, 1), pairs(wq_f, 1), wide(cos_t), ALU.mult))
            step(dve.tensor_tensor(pairs(rot, 0), pairs(rot, 0), pairs(rot2, 0), ALU.subtract))
            step(dve.tensor_tensor(pairs(rot, 1), pairs(rot, 1), pairs(rot2, 1), ALU.add))
            full = twice(rot[:, :], HEADS)
            step(dve.tensor_copy(g["wq_hi"][:, :, :, :], full))
            step(dve.tensor_tensor(g["wq_lo"][:, :, :, :], full, g["wq_hi"][:, :, :, :].bitcast(F32), ALU.subtract))
            dve.wait_ge(b_in, 32)
            with nc.vector.Fori(0, NC) as i:
                for k in range(KD):
                    dve.wait_ge(ct_hi_done.sem, ct_hi_done.at(i, k + 1))
                    dve.tensor_tensor(ct_lo[:, k, :], v_bank(k), ct_hi[:, k, :].bitcast(F32), ALU.subtract)\
                        .then_inc(v_free.sem, 1)
                for m in range(KH):
                    dve.wait_ge(hid_made.sem, hid_made.at(i, m + 1))
                    dve.tensor_copy(hid_hi[:, m, :], hid[:, m % 2, :]).then_inc(hid_hi_done.sem, 1)
                    dve.wait_ge(hid_hi_done.sem, hid_hi_done.at(i, m + 1))
                    dve.tensor_tensor(hid_lo[:, m, :], hid[:, m % 2, :], hid_hi[:, m, :].bitcast(F32), ALU.subtract)\
                        .then_inc(hid_split.sem, 1)
                dve.wait_ge(stored, stores.at(i, 0))
                for n in range(2):
                    dve.wait_ge(row_full.sem, row_full.at(i, n + 1))
                    ins = dve.tensor_tensor(made[:, 2 * n:2 * n + 2, :],
                                            v_bank(n).rearrange("p (t n) -> p t n", t=2),
                                            b2_row[:, :].unsqueeze(1).broadcast_to([P, 2, DIM]), ALU.add)
                    ins.then_inc(v_free.sem, 1)

        @block.tensor
        def _(pe):
            pe.sem_inc(rows_free.sem, 1)
            pe.wait_ge(ident_done, 1)
            with nc.tensor.Fori(0, NC) as i:
                pe.wait_ge(rows_in, rows_got.at(i, 16))
                for k in range(KD):
                    pe.wait_ge(v_free.sem, v_free.at(i, v_wait[f"ct{k}"]))
                    for t in range(NT):
                        mm = pe.transpose(v_bank(k)[:, t * P:(t + 1) * P], rows[:, t, k * P:(k + 1) * P], ident[:, :])
                    mm.then_inc(ct_full.sem, 1)
                pe.wait_ge(v_free.sem, v_free.at(i, 2))
                pe.sem_inc(rows_free.sem, 1)
                pe.wait_ge(w_done, 2)
                for m in range(KH):
                    pe.wait_ge(hid_made.sem, hid_made.at(i, a_wait[m]))
                    products = [(w, c) for k in range(KD) for w, c in ((w1_hi[:, k, :], ct_hi[:, k, :]),
                                                                      (w1_lo[:, k, :], ct_hi[:, k, :]),
                                                                      (w1_hi[:, k, :], ct_lo[:, k, :]))]
                    for n, (w, c) in enumerate(products):
                        mm = pe.matmul(a_bank(m % 3), w[:, m * P:(m + 1) * P], c, start=n == 0, stop=n == len(products) - 1)
                    mm.then_inc(hid_full.sem, 1)
                pe.wait_ge(w_done, 4)
                pe.wait_ge(hid_split.sem, hid_split.at(i, KH))
                for n in range(2):
                    pe.wait_ge(v_free.sem, v_free.at(i, v_wait[f"row{n}"]))
                    for t in (2 * n, 2 * n + 1):
                        dst = v_bank(n)[:, (t % 2) * DIM:(t % 2 + 1) * DIM]
                        for m in range(KH):
                            hh, hl = hid_hi[:, m, t * P:(t + 1) * P], hid_lo[:, m, t * P:(t + 1) * P]
                            pe.matmul(dst, hh, w2_hi[:, m, :], start=m == 0, stop=False)
                            pe.matmul(dst, hh, w2_lo[:, m, :], start=False, stop=False)
                            mm = pe.matmul(dst, hl, w2_hi[:, m, :], start=False, stop=m == KH - 1)
                    mm.then_inc(row_full.sem, 1)


def layer(nc, part, env):
    g = env
    ident, causal, slope, a_bank, v_bank, score_ps, turn_ps = (g["ident"], g["causal"], g["slope"], g["a_bank"], g["v_bank"],
                                                               g["score_ps"], g["turn_ps"])

    def sem(name):
        return part.enter_context(nc.semaphore(name))

    def sb(name, shape, dt=F32):
        return part.enter_context(nc.sbuf_tensor(name, shape, dt))

    idx = sb("idx", [P, NT], I32)
    rows = sb("token_rows", [P, NT, DIM])
    h = sb("h", [P, NT, DIM])
    xn = sb("xn", [P, NT, DIM])
    stats, mv = sb("stats", [P, NT, 6]), sb("mv", [P, NT, 2])
    var, guess, tmp = sb("var", [P, NT]), sb("guess", [P, NT]), sb("tmp", [P, NT])
    minus_half = sb("minus_half", [P, NT])
    xt_hi, xt_lo = sb("xt_hi", [P, KD, T], F32R), sb("xt_lo", [P, KD, T], F32R)
    vz = sb("vz", [P, NT, KVH, 3 * D])
    k_hi, k_lo = sb("k_hi", [P, 2, T], F32R), sb("k_lo", [P, 2, T], F32R)
    q_both = sb("q_both", [P, 3, T], F32R)
    probs = sb("probs", [P, 2, TRI])
    least, sums, recip = sb("least", [P, 2, NT]), sb("sums", [P, 2, NT]), sb("recip", [P, 2, NT])
    turned_sb = sb("turned_sb", [P, 2, TRI])
    o_hi, o_lo = sb("o_hi", [P, PAIRS, T], F32R), sb("o_lo", [P, PAIRS, T], F32R)
    rank_both = sb("rank_both", [P, T], F32R)
    ff = sb("ff", [P, 2, T])
    ff_hi, ff_lo = sb("ff_hi", [P, 2, T], F32R), sb("ff_lo", [P, 2, T], F32R)
    z_hi, z_lo = sb("z_hi", [P, T], F32R), sb("z_lo", [P, T], F32R)
    result = sb("result", [P, NT, DIM])

    def group_at(n):
        return (n + 3) // REP if (n + 3) % REP == 0 and n + 3 < HEADS else 0

    head_uses, head_released = [], []
    for n in range(HEADS + 2):
        if group_at(n):
            head_uses.append((f"k{group_at(n)}", 0))
        if n + 3 < HEADS:
            head_uses.append((f"q{n + 3}", 0))
        if n % 2 == 1 and n < HEADS:
            head_uses.append((f"o{n // 2}", 1))
        if n + 2 < HEADS:
            head_released.append(f"q{n + 2}")
        if group_at(n):
            head_released.append(f"k{group_at(n)}")
        if n >= 3 and n % 2 == 1:
            head_released.append(f"o{(n - 3) // 2}")
    before = [("x0", 0), ("x1", 1), ("v0", 0), ("v1", 1), ("k0", 0), ("q0", 1), ("q1", 0), ("q2", 0)]
    after = [("w0", 0), ("w1", 1), ("y0", 0), ("y1", 1), ("u", 0), ("z", 1), ("d0", 0), ("d1", 1)]
    v_uses = before + head_uses + after
    v_released = [n for n, _ in before[:-1]] + head_released + [n for n, _ in after]
    v_wait = bank_waits(v_uses, v_released)
    v_order = {n: k + 1 for k, n in enumerate(v_released)}
    v_bank_of = {n: b for n, b in v_uses}

    start = sem("start")
    idx_in, rows_in, stored = Count(sem("idx_in"), 16), Count(sem("rows_in"), 16 * NT), Count(sem("stored"), 16, 16)
    rows_used = Count(sem("rows_used"), 1, 1)
    v_step_sem = sem("v_steps")
    v_carry, pool_carry = sem("v_carry"), sem("pool_carry")
    var_done, guess_done, xn_done = Count(sem("var_done"), 2), Count(sem("guess_done"), 2), Count(sem("xn_done"), 2)
    xt_full, xt_hi_done = Count(sem("xt_full"), 4), Count(sem("xt_hi_done"), 4)
    v_free = Count(sem("v_bank_free"), len(v_released), 2)
    v_full = Count(sem("v_full"), 2)
    qk_full, qk_hi_done = Count(sem("qk_full"), HEADS + KVH), Count(sem("qk_hi_done"), HEADS + KVH)
    scored, biased = Count(sem("scored"), BANKS * HEADS), Count(sem("biased"), NT * HEADS, 1)
    exped, normed = Count(sem("exped"), NT * HEADS), Count(sem("normed"), HEADS)
    turned, moved, valued = Count(sem("turned"), HEADS), Count(sem("moved"), HEADS, 1), Count(sem("valued"), HEADS)
    o_hi_done, wo_full = Count(sem("o_hi_done"), PAIRS), Count(sem("wo_full"), 2)
    rank_full, rank_hi_done = Count(sem("rank_full"), 1), Count(sem("rank_hi_done"), 1)
    ff_full, ff_made, ff_hi_done = Count(sem("ff_full"), KF), Count(sem("ff_made"), KF), Count(sem("ff_hi_done"), KF)
    ff_split, ff_used = Count(sem("ff_split"), KF, 2), Count(sem("ff_used"), KF, 2)
    z_hi_done, d_full = Count(sem("z_hi_done"), 1), Count(sem("d_full"), 2)

    qk = [n for n, _ in v_uses if n[0] in "kq"]
    qk_order = {n: k + 1 for k, n in enumerate(qk)}
    qk_hi_order = {n: k + 1 for k, n in enumerate(n for n in v_released if n[0] in "kq")}

    with nc.Block() as block:
        @block.sync
        def _(sp):
            sp.sem_inc(stored.sem, 16)
            with nc.sync.Fori(0, B) as i:
                sp.wait_ge(v_free.sem, v_free.at(i, v_order["d1"]))
                sp.dma_start(g["out"][bass.ds(i, 1), :, :].rearrange("a (t p) n -> p (a t) n", p=P), result[:, :, :])\
                    .then_inc(stored.sem, 16)
            sp.wait_ge(stored.sem, 16 * B + 16)

        @block.gpsimd
        def _(pool):
            pool.memset(minus_half[:, :], -0.5).then_inc(start, 1)
            pool.memset(vz[:, :, :, :], 0.0).then_inc(start, 1)
            pool.wait_ge(start, 2)
            with nc.gpsimd.Fori(0, B) as i:
                pool.wait_ge(rows_used.sem, rows_used.at(i, 0))
                pool.sem_inc(pool_carry, 1)
                pool.dma_start(idx[:, :], g["x"][bass.ds(i, 1), :].rearrange("a (t p) -> p (a t)", p=P),
                               allow_slow_non_contiguous=True).then_inc(idx_in.sem, 16)
                pool.wait_ge(idx_in.sem, idx_in.at(i, 16))
                pool.sem_inc(pool_carry, 1)
                for t in range(NT):
                    pool.indirect_dma_start(out=rows[:, t, :], out_offset=None, in_=g["table"],
                                            in_offset=bass.IndirectOffsetOnAxis(ap=idx[:, t:t + 1].bitcast(U32), axis=0),
                                            bounds_check=ROWS - 1).then_inc(rows_in.sem, 16)
                for n in range(2):
                    pool.wait_ge(var_done.sem, var_done.at(i, n + 1))
                    pool.tensor_tensor(guess[:, :], var[:, :], minus_half[:, :], ALU.pow).then_inc(guess_done.sem, 1)

        @block.scalar
        def _(act):
            act.sem_inc(moved.sem, 1)
            with nc.scalar.Fori(0, B) as i:
                def x_high(n):
                    for k in range(KD):
                        act.wait_ge(xt_full.sem, xt_full.at(i, KD * n + k + 1))
                        act.activation(xt_hi[:, k, :], v_bank(k), ACT.Copy).then_inc(xt_hi_done.sem, 1)

                def qk_high(name):
                    n = int(name[1:])
                    dst = k_hi[:, n % 2, :] if name[0] == "k" else q_both[:, n % 3, :]
                    act.wait_ge(qk_full.sem, qk_full.at(i, qk_order[name]))
                    act.activation(dst, v_bank(v_bank_of[name]), ACT.Copy).then_inc(qk_hi_done.sem, 1)

                def exps(n):
                    for m, q in enumerate(Q_ORDER):
                        act.wait_ge(biased.sem, biased.at(i, NT * n + m + 1))
                        at = probs[:, n % 2, Q_AT[q]:Q_AT[q] + P * (q + 1)]
                        act.activation(at, at, ACT.Exp, bias=least[:, n % 2, q:q + 1], scale=-1.0,
                                       accum_out=sums[:, n % 2, q:q + 1]).then_inc(exped.sem, 1)

                def move(n):
                    act.wait_ge(turned.sem, turned.at(i, n + 1))
                    act.activation(turned_sb[:, n % 2, :], turn_ps, ACT.Copy).then_inc(moved.sem, 1)

                def o_high(j):
                    act.wait_ge(valued.sem, valued.at(i, 2 * j + 2))
                    act.activation(o_hi[:, j, :], v_bank(v_bank_of[f"o{j}"]), ACT.Copy).then_inc(o_hi_done.sem, 1)

                x_high(0)
                for name in ("k0", "q0", "q1"):
                    qk_high(name)
                exps(0)
                for n in range(HEADS + 2):
                    if n + 2 < HEADS:
                        qk_high(f"q{n + 2}")
                    if group_at(n):
                        qk_high(f"k{group_at(n)}")
                    if n >= 3 and n % 2 == 1:
                        o_high((n - 3) // 2)
                    if n + 1 < HEADS:
                        exps(n + 1)
                    if n < HEADS:
                        move(n)
                x_high(1)
                act.wait_ge(rank_full.sem, rank_full.at(i, 1))
                act.activation(rank_both[:, :], v_bank(v_bank_of["u"]), ACT.Copy).then_inc(rank_hi_done.sem, 1)
                for f in range(KF):
                    act.wait_ge(ff_split.sem, ff_split.at(i, f - 1))
                    act.wait_ge(ff_full.sem, ff_full.at(i, f + 1))
                    act.activation(ff[:, f % 2, :], a_bank(f % 3), ACT.Gelu_apprx_tanh, bias=g["c1_col"][:, f:f + 1])\
                        .then_inc(ff_made.sem, 1)
                act.wait_ge(ff_used.sem, ff_used.at(i, KF))
                act.activation(z_hi[:, :], v_bank(v_bank_of["z"]), ACT.Copy).then_inc(z_hi_done.sem, 1)

        @block.vector
        def _(dve):
            dve.sem_inc(v_free.sem, 2)
            dve.sem_inc(rows_used.sem, 1)
            dve.sem_inc(biased.sem, 1)
            dve.sem_inc(ff_split.sem, 2)
            PER_TURN = 2 * (4 + 3) + 2 + 2 * HEADS
            v_steps = Count(v_step_sem, PER_TURN)
            dve.wait_ge(start, 2)
            with nc.vector.Fori(0, B) as i:
                done = [0]

                def step(ins):
                    done[0] += 1
                    ins.then_inc(v_steps.sem, 1)

                def stepped():
                    dve.wait_ge(v_steps.sem, v_steps.at(i, done[0]))

                def norm(src, n):
                    for t in range(NT):
                        ins = dve.bn_stats(stats[:, t, :], src[:, t, :])
                    step(ins)
                    stepped()
                    dve.sem_inc(v_carry, 1)
                    for t in range(NT):
                        ins = dve.bn_aggr(mv[:, t, :], stats[:, t, :])
                    step(ins)
                    stepped()
                    dve.tensor_scalar(var[:, :], mv[:, :, 1], EPS, None, ALU.add).then_inc(var_done.sem, 1)
                    dve.wait_ge(guess_done.sem, guess_done.at(i, n + 1))
                    step(dve.tensor_tensor(tmp[:, :], guess[:, :], guess[:, :], ALU.mult))
                    stepped()
                    step(dve.tensor_tensor(tmp[:, :], tmp[:, :], var[:, :], ALU.mult))
                    stepped()
                    step(dve.tensor_scalar(tmp[:, :], tmp[:, :], -0.5, 1.5, ALU.mult, ALU.add))
                    stepped()
                    step(dve.tensor_tensor(guess[:, :], guess[:, :], tmp[:, :], ALU.mult))
                    stepped()
                    for t in range(NT):
                        ins = dve.tensor_scalar(xn[:, t, :], src[:, t, :], mv[:, t, 0:1], guess[:, t:t + 1],
                                                ALU.subtract, ALU.mult)
                    step(ins)
                    stepped()

                def x_low(n):
                    for k in range(KD):
                        dve.wait_ge(xt_hi_done.sem, xt_hi_done.at(i, KD * n + k + 1))
                        dve.tensor_tensor(xt_lo[:, k, :], v_bank(k), xt_hi[:, k, :].bitcast(F32), ALU.subtract)\
                            .then_inc(v_free.sem, 1)

                def qk_low(name):
                    n = int(name[1:])
                    dve.wait_ge(qk_hi_done.sem, qk_hi_done.at(i, qk_hi_order[name]))
                    bank = v_bank(v_bank_of[name])
                    if name[0] == "k":
                        ins = dve.tensor_tensor(k_lo[:, n % 2, :], bank, k_hi[:, n % 2, :].bitcast(F32), ALU.subtract)
                    else:
                        half = q_both[D:P, n % 3, :]
                        ins = dve.tensor_tensor(half, bank[D:P, :], half.bitcast(F32), ALU.subtract)
                    ins.then_inc(v_free.sem, 1)

                def bias_scores(n):
                    for m, q in enumerate(Q_ORDER):
                        at = slice(Q_AT[q], Q_AT[q] + P * (q + 1))
                        if q != 0:
                            dve.wait_ge(scored.sem, scored.at(i, BANKS * n + Q_BANK[q]))
                            dve.sem_inc(v_carry, 1)
                        dve.tensor_tensor_reduce(out=probs[:, n % 2, at], in0=score_ps[:, at], in1=causal[:, at],
                                                 scale=slope[:, n:n + 1], scalar=3e38, op0=ALU.add, op1=ALU.min,
                                                 accum_out=least[:, n % 2, q:q + 1]).then_inc(biased.sem, 1)

                def normalize(n):
                    dve.wait_ge(exped.sem, exped.at(i, NT * (n + 1)))
                    step(dve.tensor_scalar(recip[:, n % 2, :], sums[:, n % 2, :], 1.0, None, ALU.add))
                    stepped()
                    step(dve.reciprocal(recip[:, n % 2, :], recip[:, n % 2, :]))
                    stepped()
                    for q in Q_ORDER:
                        at = probs[:, n % 2, Q_AT[q]:Q_AT[q] + P * (q + 1)]
                        ins = dve.tensor_scalar(at, at, recip[:, n % 2, q:q + 1], None, ALU.mult)
                    ins.then_inc(normed.sem, 1)

                def o_low(j):
                    dve.wait_ge(o_hi_done.sem, o_hi_done.at(i, j + 1))
                    dve.tensor_tensor(o_lo[:, j, :], v_bank(v_bank_of[f"o{j}"]), o_hi[:, j, :].bitcast(F32),
                                      ALU.subtract).then_inc(v_free.sem, 1)

                def two_tiles(t, n):
                    return t[:, 2 * n:2 * n + 2, :]

                dve.wait_ge(rows_in.sem, rows_in.at(i, 16 * NT))
                norm(rows, 0)
                dve.sem_inc(xn_done.sem, 1)
                step(dve.tensor_copy(h[:, :, :], rows[:, :, :]))
                stepped()
                dve.sem_inc(rows_used.sem, 1)
                x_low(0)
                for n in range(2):
                    dve.wait_ge(v_full.sem, v_full.at(i, n + 1))
                    dve.tensor_copy(vz[:, 2 * n:2 * n + 2, :, D:2 * D],
                                    v_bank(n).rearrange("p (t g d) -> p t g d", t=2, g=KVH)).then_inc(v_free.sem, 1)
                for name in ("k0", "q0", "q1"):
                    qk_low(name)
                bias_scores(0)
                normalize(0)
                for n in range(HEADS + 2):
                    if n + 2 < HEADS:
                        qk_low(f"q{n + 2}")
                    if group_at(n):
                        qk_low(f"k{group_at(n)}")
                    if n >= 3 and n % 2 == 1:
                        o_low((n - 3) // 2)
                    if n + 1 < HEADS:
                        bias_scores(n + 1)
                        normalize(n + 1)
                for n in range(2):
                    dve.wait_ge(wo_full.sem, wo_full.at(i, n + 1))
                    dve.tensor_tensor(two_tiles(h, n), v_bank(n).rearrange("p (t n) -> p t n", t=2), two_tiles(h, n),
                                      ALU.add).then_inc(v_free.sem, 1)
                dve.wait_ge(v_free.sem, v_free.at(i, v_order["w1"]))
                norm(h, 1)
                dve.sem_inc(xn_done.sem, 1)
                step(dve.tensor_tensor(h[:, :, :], h[:, :, :], g["c2_row"][:, :].unsqueeze(1).broadcast_to([P, NT, DIM]),
                                       ALU.add))
                x_low(1)
                dve.wait_ge(rank_hi_done.sem, rank_hi_done.at(i, 1))
                dve.tensor_tensor(rank_both[D:P, :], v_bank(v_bank_of["u"])[D:P, :], rank_both[D:P, :].bitcast(F32),
                                  ALU.subtract).then_inc(v_free.sem, 1)
                for f in range(KF):
                    dve.wait_ge(ff_used.sem, ff_used.at(i, f - 1))
                    dve.wait_ge(ff_made.sem, ff_made.at(i, f + 1))
                    dve.tensor_copy(ff_hi[:, f % 2, :], ff[:, f % 2, :]).then_inc(ff_hi_done.sem, 1)
                    dve.wait_ge(ff_hi_done.sem, ff_hi_done.at(i, f + 1))
                    dve.tensor_tensor(ff_lo[:, f % 2, :], ff[:, f % 2, :], ff_hi[:, f % 2, :].bitcast(F32),
                                      ALU.subtract).then_inc(ff_split.sem, 1)
                dve.wait_ge(z_hi_done.sem, z_hi_done.at(i, 1))
                dve.tensor_tensor(z_lo[:, :], v_bank(v_bank_of["z"]), z_hi[:, :].bitcast(F32), ALU.subtract)\
                    .then_inc(v_free.sem, 1)
                dve.wait_ge(stored.sem, stored.at(i, 0))
                for n in range(2):
                    dve.wait_ge(d_full.sem, d_full.at(i, n + 1))
                    dve.tensor_tensor(two_tiles(result, n), v_bank(n).rearrange("p (t n) -> p t n", t=2),
                                      two_tiles(h, n), ALU.add).then_inc(v_free.sem, 1)
                assert done[0] == PER_TURN, done[0]

        @block.tensor
        def _(pe):
            pe.sem_inc(ff_used.sem, 2)
            with nc.tensor.Fori(0, B) as i:
                def open_bank(name):
                    pe.wait_ge(v_free.sem, v_free.at(i, v_wait[name]))
                    return v_bank(v_bank_of[name])

                def evacuated(name):
                    pe.wait_ge(v_free.sem, v_free.at(i, v_order[name]))

                def turn_rows(names, n):
                    pe.wait_ge(xn_done.sem, xn_done.at(i, n + 1))
                    for k, name in enumerate(names):
                        dst = open_bank(name)
                        for t in range(NT):
                            mm = pe.transpose(dst[:, t * P:(t + 1) * P], xn[:, t, k * P:(k + 1) * P], ident[:, :])
                        mm.then_inc(xt_full.sem, 1)
                    evacuated(names[-1])

                def three(dst, pairs):
                    parts = [x for (wh, wl), (xh, xl) in pairs for x in ((wh, xh), (wl, xh), (wh, xl))]
                    for n, (w, x) in enumerate(parts):
                        mm = pe.matmul(dst, w, x, start=n == 0, stop=n == len(parts) - 1)
                    return mm

                def both(w, n):
                    return w[:, n, :, :].rearrange("p a d -> p (a d)")

                def qk_product(name):
                    n = int(name[1:])
                    hi, lo = (g["wk_hi"], g["wk_lo"]) if name[0] == "k" else (g["wq_hi"], g["wq_lo"])
                    dst = open_bank(name)
                    three(dst, [((both(hi, n), both(lo, n)), (xt_hi[:, 1, :], xt_lo[:, 1, :]))])\
                        .then_inc(qk_full.sem, 1)

                def scores(n):
                    evacuated(f"q{n}")
                    pe.wait_ge(biased.sem, biased.at(i, NT * n))
                    for q in Q_ORDER:
                        dst = score_ps[:, Q_AT[q]:Q_AT[q] + P * (q + 1)]
                        w = q_both[:, n % 3, q * P:(q + 1) * P]
                        slot = n // REP % 2
                        pe.matmul(dst, w, k_hi[:, slot, 0:P * (q + 1)], start=True, stop=False)
                        mm = pe.matmul(dst, w, k_lo[:, slot, 0:P * (q + 1)], start=False, stop=True)
                        if q != 2:
                            mm.then_inc(scored.sem, 1)

                def turn(n):
                    pe.wait_ge(normed.sem, normed.at(i, n + 1))
                    pe.wait_ge(moved.sem, moved.at(i, n))
                    for k in range(NT):
                        for q in range(k, NT):
                            mm = pe.transpose(turn_ps[:, K_AT[k] + P * (q - k):K_AT[k] + P * (q - k + 1)],
                                              probs[:, n % 2, Q_AT[q] + P * k:Q_AT[q] + P * (k + 1)], ident[:, :])
                    mm.then_inc(turned.sem, 1)

                def values(n):
                    name = f"o{n // 2}"
                    if n % 2 == 0:
                        open_bank(name)
                    pe.wait_ge(moved.sem, moved.at(i, n + 1))
                    dst = v_bank(v_bank_of[name])
                    at = slice(D, 3 * D) if n % 2 == 0 else slice(0, 2 * D)
                    for k in range(NT):
                        mm = pe.matmul(dst[:, P * k:T], vz[:, k, n // REP, at],
                                       turned_sb[:, n % 2, K_AT[k]:K_AT[k] + T - P * k],
                                       start=n % 2 == 0 and k == 0, stop=n % 2 == 1 and k == NT - 1,
                                       skip_group_check=True)
                    mm.then_inc(valued.sem, 1)

                turn_rows(("x0", "x1"), 0)
                for n in range(2):
                    dst = open_bank(f"v{n}")
                    for t in (2 * n, 2 * n + 1):
                        tok = slice(t * P, (t + 1) * P)
                        mm = three(dst[:, (t % 2) * DIM:(t % 2 + 1) * DIM],
                                   [((xt_hi[:, 0, tok], xt_lo[:, 0, tok]), (g["wv_hi"][:, :], g["wv_lo"][:, :]))])
                    mm.then_inc(v_full.sem, 1)
                for name in ("k0", "q0", "q1"):
                    qk_product(name)
                scores(0)
                qk_product("q2")
                for n in range(HEADS + 1):
                    if group_at(n):
                        qk_product(f"k{group_at(n)}")
                    if n + 1 < HEADS:
                        scores(n + 1)
                    if n < HEADS:
                        turn(n)
                    if n + 3 < HEADS:
                        qk_product(f"q{n + 3}")
                    if n >= 1:
                        values(n - 1)
                evacuated(f"o{PAIRS - 1}")
                for n in range(2):
                    dst = open_bank(f"w{n}")
                    for t in (2 * n, 2 * n + 1):
                        tok = slice(t * P, (t + 1) * P)
                        mm = three(dst[:, (t % 2) * DIM:(t % 2 + 1) * DIM],
                                   [((o_hi[:, j, tok], o_lo[:, j, tok]), (g["wo_hi"][:, j, :], g["wo_lo"][:, j, :]))
                                    for j in range(PAIRS)])
                    mm.then_inc(wo_full.sem, 1)
                turn_rows(("y0", "y1"), 1)
                three(open_bank("u"), [((both(g["u1_hi"], k), both(g["u1_lo"], k)), (xt_hi[:, k, :], xt_lo[:, k, :]))
                                       for k in range(KD)]).then_inc(rank_full.sem, 1)
                evacuated("u")
                z = open_bank("z")
                for f in range(KF + 1):
                    if f < KF:
                        cols = slice(f * P, (f + 1) * P)
                        pe.matmul(a_bank(f % 3), g["v1_hi"][:, cols], rank_both[:, :], start=True, stop=False)
                        pe.matmul(a_bank(f % 3), g["v1_lo"][:, cols], rank_both[:, :], start=False, stop=True)\
                            .then_inc(ff_full.sem, 1)
                    if f >= 1:
                        e = f - 1
                        pe.wait_ge(ff_split.sem, ff_split.at(i, e + 1))
                        pe.matmul(z, g["u2_both"][:, e, :], ff_hi[:, e % 2, :], start=e == 0, stop=False, skip_group_check=True)
                        pe.matmul(z, g["u2_both"][:, e, :], ff_lo[:, e % 2, :], start=False, stop=e == KF - 1,
                                  skip_group_check=True).then_inc(ff_used.sem, 1)
                evacuated("z")
                for n in range(2):
                    dst = open_bank(f"d{n}")
                    for t in (2 * n, 2 * n + 1):
                        tok = slice(t * P, (t + 1) * P)
                        mm = three(dst[:, (t % 2) * DIM:(t % 2 + 1) * DIM],
                                   [((z_hi[:, tok], z_lo[:, tok]), (g["v2_hi"][:, :], g["v2_lo"][:, :]))])
                    mm.then_inc(d_full.sem, 1)


_INS = ["x", "L0_tok_codebook", "L0_tok_W1", "L0_tok_b1", "L0_tok_W2", "L0_tok_b2", "L0_attn_Wq", "L0_attn_Wk",
        "L0_attn_Wv", "L0_attn_Wo", "L0_attn_q_phase_angle", "L0_attn_alibi_log_slopes", "L0_ffn_U1", "L0_ffn_V1",
        "L0_ffn_b1", "L0_ffn_U2", "L0_ffn_V2", "L0_ffn_b2"]
_OUT = ((B, T, DIM), "float32")


def kernel(**inputs):
    import numpy as _np
    import concourse.bacc as _bacc
    from concourse import mybir as _mybir
    from concourse.bass_utils import run_bass_kernel_spmd as _run

    nc = _bacc.Bacc("TRN2", target_bir_lowering=False, num_devices=1)
    arrays, args = {}, []
    for name in _INS:
        a = _np.ascontiguousarray(inputs[name])
        arrays[f"in_{name}_dram"] = a
        args.append(nc.dram_tensor(f"in_{name}_dram", a.shape, _mybir.dt.from_np(a.dtype), kind="ExternalInput").ap())
    shape, dtype = _OUT
    args.append(nc.dram_tensor("out_dram", shape, _mybir.dt.from_np(_np.dtype(dtype)), kind="ExternalOutput").ap())
    lm_tower(nc, *args)
    r = _run(nc, [arrays], core_ids=[0])
    return r.results[0]["out_dram"]
```
